# Optimizing a Trainium2 kernel written in Bass

```python
import numpy as np
import jax
import jax.numpy as jnp

def _softmax(x, axis=-1):
    return jax.nn.softmax(x, axis=axis)
def _gelu(x):
    return jax.nn.gelu(x, approximate=True)
def _silu(x):
    return jax.nn.silu(x)
def _sigmoid(x):
    return jax.nn.sigmoid(x)
def _layernorm(x, axis=-1, eps=1e-5):
    m = jnp.mean(x, axis=axis, keepdims=True)
    v = jnp.var(x, axis=axis, keepdims=True)
    return (x - m) / jnp.sqrt(v + eps)
def _scatter_add(tgt, idx, src, axis=0):
    return tgt.at[idx].add(src)
def _segment_sum(src, seg, n):
    return jax.ops.segment_sum(src, seg, n)

kernel_name = 'mk_conv_preact_d2_conv_nhwc768_6defe4'

def setup_inputs(seed: int = 0):
    np.random.seed(seed)
    _w = jnp.asarray
    def _rec_inputs():
        import jax
        import jax.numpy as jnp
        _gk = jax.random.key(seed)
        x = -0.0008768 + 1.001 * jax.random.normal(jax.random.fold_in(_gk, 1), (1, 48, 48, 768), jnp.float32)
        return x
    x = _rec_inputs()
    def _L0_conv_setup():
        import jax, jax.numpy as jnp
        import numpy as np
        B, Hs, Ws, DIM = (1, 48, 48, 768)
        NUM_HEADS, HEAD_DIM = (12, 64)
        RANK, ALPHA = (4, 1.0)
        SCALING = ALPHA / RANK
        SCALE = HEAD_DIM ** (-0.5)

        def _get_rel_pos(size, rel_pos):
            coords = jnp.arange(size)
            idx = coords[:, None] - coords[None, :] + (size - 1)
            return rel_pos[idx]
        key = jax.random.key(seed)
        ks = jax.random.split(key, 13)
        s = lambda k, shape, sc=0.02: jax.random.normal(k, shape, jnp.float32) * sc
        return dict(x=jax.random.normal(ks[0], (B, Hs, Ws, DIM), jnp.float32), qkv_w=s(ks[1], (3 * DIM, DIM)), qkv_b=s(ks[2], (3 * DIM,)), proj_w=s(ks[3], (DIM, DIM)), proj_b=s(ks[4], (DIM,)), rel_pos_h=s(ks[5], (2 * Hs - 1, HEAD_DIM)), rel_pos_w=s(ks[6], (2 * Ws - 1, HEAD_DIM)), lora_q_A=s(ks[7], (RANK, DIM)), lora_q_B=s(ks[8], (DIM, RANK)), lora_k_A=s(ks[9], (RANK, DIM)), lora_k_B=s(ks[10], (DIM, RANK)), lora_v_A=s(ks[11], (RANK, DIM)), lora_v_B=s(ks[12], (DIM, RANK)))
    _L0_conv_all = _L0_conv_setup()
    _L0_conv_in = {k: v for k, v in _L0_conv_all.items() if k in ('qkv_w', 'qkv_b', 'proj_w', 'proj_b', 'rel_pos_h', 'rel_pos_w', 'lora_q_A', 'lora_q_B', 'lora_k_A', 'lora_k_B', 'lora_v_A', 'lora_v_B', )}
    del _L0_conv_all

    def _L1_conv_setup():
        import jax, jax.numpy as jnp
        import numpy as np
        H_PATCH, W_PATCH = (48, 48)
        EMBED_DIM = 768
        VALUE_DIM = 768
        NUM_HEADS = 12
        KEY_DIM = EMBED_DIM // NUM_HEADS
        HEAD_DIM = VALUE_DIM // NUM_HEADS
        SCALING = KEY_DIM ** (-0.5)
        key = jax.random.key(seed)
        ks = jax.random.split(key, 10)
        B = 4
        N = H_PATCH * W_PATCH
        x = jax.random.normal(ks[0], (B, H_PATCH, W_PATCH, EMBED_DIM), dtype=jnp.float32)
        decay = jax.random.uniform(ks[1], (NUM_HEADS, N, N), dtype=jnp.float32)
        s = EMBED_DIM ** (-0.5)
        Wq = jax.random.normal(ks[2], (EMBED_DIM, EMBED_DIM), dtype=jnp.float32) * s
        bq = jnp.zeros((EMBED_DIM,), dtype=jnp.float32)
        Wk = jax.random.normal(ks[3], (EMBED_DIM, EMBED_DIM), dtype=jnp.float32) * s
        bk = jnp.zeros((EMBED_DIM,), dtype=jnp.float32)
        Wv = jax.random.normal(ks[4], (VALUE_DIM, EMBED_DIM), dtype=jnp.float32) * s
        bv = jnp.zeros((VALUE_DIM,), dtype=jnp.float32)
        Wo = jax.random.normal(ks[5], (EMBED_DIM, VALUE_DIM), dtype=jnp.float32) * VALUE_DIM ** (-0.5)
        bo = jnp.zeros((EMBED_DIM,), dtype=jnp.float32)
        return {'x': x, 'decay': decay, 'Wq': Wq, 'bq': bq, 'Wk': Wk, 'bk': bk, 'Wv': Wv, 'bv': bv, 'Wo': Wo, 'bo': bo}
    _L1_conv_all = _L1_conv_setup()
    _L1_conv_in = {k: v for k, v in _L1_conv_all.items() if k in ('decay', 'Wq', 'bq', 'Wk', 'bk', 'Wv', 'bv', 'Wo', 'bo', )}
    del _L1_conv_all

    return {
        "x": x,
        "L0_conv_qkv_w": _L0_conv_in["qkv_w"],
        "L0_conv_qkv_b": _L0_conv_in["qkv_b"],
        "L0_conv_proj_w": _L0_conv_in["proj_w"],
        "L0_conv_proj_b": _L0_conv_in["proj_b"],
        "L0_conv_rel_pos_h": _L0_conv_in["rel_pos_h"],
        "L0_conv_rel_pos_w": _L0_conv_in["rel_pos_w"],
        "L0_conv_lora_q_A": _L0_conv_in["lora_q_A"],
        "L0_conv_lora_q_B": _L0_conv_in["lora_q_B"],
        "L0_conv_lora_k_A": _L0_conv_in["lora_k_A"],
        "L0_conv_lora_k_B": _L0_conv_in["lora_k_B"],
        "L0_conv_lora_v_A": _L0_conv_in["lora_v_A"],
        "L0_conv_lora_v_B": _L0_conv_in["lora_v_B"],
        "L1_conv_decay": _L1_conv_in["decay"],
        "L1_conv_Wq": _L1_conv_in["Wq"],
        "L1_conv_bq": _L1_conv_in["bq"],
        "L1_conv_Wk": _L1_conv_in["Wk"],
        "L1_conv_bk": _L1_conv_in["bk"],
        "L1_conv_Wv": _L1_conv_in["Wv"],
        "L1_conv_bv": _L1_conv_in["bv"],
        "L1_conv_Wo": _L1_conv_in["Wo"],
        "L1_conv_bo": _L1_conv_in["bo"],
    }

def reference(x, L0_conv_qkv_w, L0_conv_qkv_b, L0_conv_proj_w, L0_conv_proj_b, L0_conv_rel_pos_h, L0_conv_rel_pos_w, L0_conv_lora_q_A, L0_conv_lora_q_B, L0_conv_lora_k_A, L0_conv_lora_k_B, L0_conv_lora_v_A, L0_conv_lora_v_B, L1_conv_decay, L1_conv_Wq, L1_conv_bq, L1_conv_Wk, L1_conv_bk, L1_conv_Wv, L1_conv_bv, L1_conv_Wo, L1_conv_bo):
    import jax
    import jax.numpy as jnp
    def _L0_conv_ref(x, qkv_w, qkv_b, proj_w, proj_b, rel_pos_h, rel_pos_w, lora_q_A, lora_q_B, lora_k_A, lora_k_B, lora_v_A, lora_v_B):
        import jax, jax.numpy as jnp
        import numpy as np
        B, Hs, Ws, DIM = (1, 48, 48, 768)
        NUM_HEADS, HEAD_DIM = (12, 64)
        RANK, ALPHA = (4, 1.0)
        SCALING = ALPHA / RANK
        SCALE = HEAD_DIM ** (-0.5)

        def _get_rel_pos(size, rel_pos):
            coords = jnp.arange(size)
            idx = coords[:, None] - coords[None, :] + (size - 1)
            return rel_pos[idx]
        Bn, Hq, Wq, dim = x.shape
        N = Hq * Wq
        x_flat = x.reshape(Bn, N, dim)
        qkv = (x_flat @ qkv_w.T + qkv_b).reshape(Bn, N, 3, NUM_HEADS, HEAD_DIM)
        qkv = jnp.transpose(qkv, (2, 0, 3, 1, 4))

        def lora(A, Bm):
            d = x_flat @ A.T @ Bm.T * SCALING
            return jnp.transpose(d.reshape(Bn, N, NUM_HEADS, HEAD_DIM), (0, 2, 1, 3))
        q = (qkv[0] + lora(lora_q_A, lora_q_B)).reshape(Bn * NUM_HEADS, N, HEAD_DIM)
        k = (qkv[1] + lora(lora_k_A, lora_k_B)).reshape(Bn * NUM_HEADS, N, HEAD_DIM)
        v = (qkv[2] + lora(lora_v_A, lora_v_B)).reshape(Bn * NUM_HEADS, N, HEAD_DIM)
        attn = q * SCALE @ jnp.swapaxes(k, -2, -1)
        Rh = _get_rel_pos(Hq, rel_pos_h)
        Rw = _get_rel_pos(Wq, rel_pos_w)
        r_q = q.reshape(Bn * NUM_HEADS, Hq, Wq, HEAD_DIM)
        rel_h = jnp.einsum('bhwc,hkc->bhwk', r_q, Rh)
        rel_w = jnp.einsum('bhwc,wkc->bhwk', r_q, Rw)
        attn = (attn.reshape(-1, Hq, Wq, Hq, Wq) + rel_h[:, :, :, :, None] + rel_w[:, :, :, None, :]).reshape(-1, N, N)
        attn = jax.nn.softmax(attn, axis=-1)
        out = (attn @ v).reshape(Bn, NUM_HEADS, Hq, Wq, HEAD_DIM)
        out = jnp.transpose(out, (0, 2, 3, 1, 4)).reshape(Bn, Hq, Wq, dim)
        return out @ proj_w.T + proj_b

    def _L1_conv_ref(x, decay, Wq, bq, Wk, bk, Wv, bv, Wo, bo):
        import jax, jax.numpy as jnp
        import numpy as np
        H_PATCH, W_PATCH = (48, 48)
        EMBED_DIM = 768
        VALUE_DIM = 768
        NUM_HEADS = 12
        KEY_DIM = EMBED_DIM // NUM_HEADS
        HEAD_DIM = VALUE_DIM // NUM_HEADS
        SCALING = KEY_DIM ** (-0.5)
        B, pH, pW, D = x.shape
        N = pH * pW
        xf = x.reshape(B, N, D)
        q = xf @ Wq.T + bq
        k = (xf @ Wk.T + bk) * SCALING
        v = xf @ Wv.T + bv
        q = q.reshape(B, N, NUM_HEADS, KEY_DIM).transpose(0, 2, 1, 3)
        k = k.reshape(B, N, NUM_HEADS, KEY_DIM).transpose(0, 2, 1, 3)
        v = v.reshape(B, N, NUM_HEADS, HEAD_DIM).transpose(0, 2, 1, 3)
        scores = jnp.einsum('bhnd,bhmd->bhnm', q, k)
        attn = jax.nn.softmax(scores, axis=-1) * decay[None]
        out = jnp.einsum('bhnm,bhmd->bhnd', attn, v)
        out = out.transpose(0, 2, 1, 3).reshape(B, N, NUM_HEADS * HEAD_DIM)
        out = out.reshape(B, pH, pW, VALUE_DIM)
        return out @ Wo.T + bo

    def _gn(v, G=32, eps=1e-5):
        B_, H_, W_, C_ = v.shape
        g = v.reshape(B_, H_, W_, G, C_ // G)
        m = jnp.mean(g, axis=(1, 2, 4), keepdims=True)
        s = jnp.var(g, axis=(1, 2, 4), keepdims=True)
        return ((g - m) / jnp.sqrt(s + eps)).reshape(v.shape)

    def _ln_c(v, eps=1e-6):
        m = jnp.mean(v, axis=-1, keepdims=True)
        s = jnp.var(v, axis=-1, keepdims=True)
        return (v - m) / jnp.sqrt(s + eps)

    def _ln_t(v, eps=1e-5):
        m = jnp.mean(v, axis=-1, keepdims=True)
        s = jnp.var(v, axis=-1, keepdims=True)
        return (v - m) / jnp.sqrt(s + eps)

    def _to_tokens(v):
        B_, H_, W_, C_ = v.shape
        return v.reshape(B_, H_ * W_, C_)
    def _from_tokens(t, like):
        return t.reshape(like.shape)

    x = x + _L0_conv_ref(_gn(x), L0_conv_qkv_w, L0_conv_qkv_b, L0_conv_proj_w, L0_conv_proj_b, L0_conv_rel_pos_h, L0_conv_rel_pos_w, L0_conv_lora_q_A, L0_conv_lora_q_B, L0_conv_lora_k_A, L0_conv_lora_k_B, L0_conv_lora_v_A, L0_conv_lora_v_B)
    x = x + _L1_conv_ref(_gn(x), L1_conv_decay, L1_conv_Wq, L1_conv_bq, L1_conv_Wk, L1_conv_bk, L1_conv_Wv, L1_conv_bv, L1_conv_Wo, L1_conv_bo)
    return x


_drawn_inputs = setup_inputs


def setup_inputs(seed=0):
    import zlib

    import numpy as np

    out = dict(_drawn_inputs(seed))
    spreads = {'L1_conv_bq': (0.0, 0.8),
     'L1_conv_bk': (0.0, 2.0),
     'L1_conv_bv': (0.0, 0.1),
     'L1_conv_bo': (0.0, 0.1)}
    factors = {'L0_conv_qkv_b': 4.62,
     'L0_conv_rel_pos_h': 32.319,
     'L0_conv_rel_pos_w': 32.214,
     'L0_conv_lora_q_A': 32.261,
     'L0_conv_lora_q_B': 32.121,
     'L0_conv_lora_k_A': 64.0,
     'L0_conv_lora_k_B': 64.0,
     'L0_conv_lora_v_A': 8.0,
     'L0_conv_lora_v_B': 8.0,
     'L1_conv_decay': 5.655}
    for name, (base, spread) in spreads.items():
        noise = np.random.default_rng([zlib.crc32(name.encode()), seed]).standard_normal(out[name].shape)
        drawn = base * np.exp(spread * noise) if base else spread * noise
        out[name] = jnp.asarray(drawn.astype(out[name].dtype))
    for name, factor in factors.items():
        out[name] = (out[name] * factor).astype(out[name].dtype)
    return out
```

```python
from contextlib import ExitStack

import numpy as np

import concourse.bass as bass
from concourse import mybir

F32 = mybir.dt.float32
F32R = mybir.dt.float32r
ALU = mybir.AluOpType
ACT = mybir.ActivationFunctionType
AX = mybir.AxisListType.X

P = 128
SIDE = 48
N = SIDE * SIDE
D = 768
H = 12
HD = D // H
KC = D // P
NT = N // P
GROUPS = 32
GC = D // GROUPS
EPS = 1e-5
SCALE = HD ** -0.5
RANK = 4
LORA_SCALE = 1.0 / RANK
W = 384
NCH = N // W
CT = W // P
HALVES = 6
OT = W // P
TAB = 2 * SIDE
UNITS = H * NT
UNROLL = 6
TURNS = UNITS // UNROLL
TPH = NT // UNROLL
SCH = 3
SC = N // SCH
QRING, BRING, PRING, TRING = 3, 3, 6, 2
LAG = 4
XLAG = 3
MLAG = 2
POOL_COLS = 14 * P
TGROUPS = [4, 4, 4, 4, 2]
BIG = 3.0e38

EVAC = {0: "ADADA", 1: "ADAAA"}

AT_CONST = 1280
AT_B = 10496
AT_A = AT_B + KC * N * 4
AT_C = AT_A + KC * N * 4
AT_D = AT_C + 77952
AT_END = AT_D + KC * D * 4


class Layer:
    pass


def program(nc, x_in, tables, lora_a, lora_b, decay, w_all, b_qkv, b_out, ident_in, avg_in, spread_in, out):
    ctx = ExitStack()
    with ctx:
        def sem(name):
            return ctx.enter_context(nc.semaphore(name))

        def at(name, shape, dt, offset):
            return nc.alloc_sbuf_tensor_at(name, shape, dt, offset=offset)

        ctx.enter_context(nc.sbuf_tensor("fence", [P, (AT_END - AT_CONST) // 4], F32))

        ident = at("ident", [P, P], F32, AT_CONST)
        avg = at("avg", [P, KC, GROUPS], F32, AT_CONST + 512)
        spread = at("spread", [GROUPS, D], F32, AT_CONST + 1280)
        small = [AT_CONST + 4352]

        def small_at(name, shape):
            here = small[0]
            small[0] += -(-int(np.prod(shape[1:])) * 4 // 32) * 32
            assert small[0] <= AT_B
            return at(name, shape, F32, here)

        bn = small_at("bn", [P, KC, NT // 2, 6])
        mv = small_at("mv", [P, KC, 2])
        mean_c = small_at("mean_c", [P, KC])
        dev = small_at("dev", [P, KC])
        spread_var = small_at("spread_var", [P, KC])
        rstd_c = small_at("rstd_c", [P, KC])
        grp = small_at("grp", [GROUPS, 8])
        bcol = small_at("bcol", [P, 3 * KC])
        pmax = small_at("pmax", [P, PRING, 4])
        nmax = small_at("nmax", [P, PRING])
        rsum = small_at("rsum", [P, PRING])
        rinv = small_at("rinv", [P, PRING])
        la = at("la", [RANK, D], F32, AT_C + 64512)

        x_hi = at("x_hi", [P, KC, N], F32R, AT_B)
        x_t = at("x_t", [P, KC, N], F32, AT_A)
        x_lo = at("x_lo", [P, KC, N], F32R, AT_A)
        w_hi = at("w_hi", [P, 2, KC, W], F32R, AT_C)
        w_lo = at("w_lo", [P, 2, KC, W], F32R, AT_C + 18432)
        stage = at("stage", [P, 2, KC, W], F32, AT_C + 36864)
        e_hi = at("e_hi", [P, OT, W], F32R, AT_C + 55296)
        e_lo = at("e_lo", [P, OT, W], F32R, AT_C + 59904)
        v_f = at("v_f", [P, OT, W], F32, AT_C + 55296)
        v_n = at("v_n", [P, OT, CT, P], F32, AT_C + 59904)
        lb = at("lb", [RANK, D], F32, AT_C + 67584)
        x_tile = at("x_tile", [P, 2, D], F32, AT_C + 70656)
        tab_f = at("tab_f", [P, 2 * TAB], F32, AT_C + 76800)
        qr_sb = at("qr_sb", [P, OT, 2 * CT, 2 * TAB], F32, AT_D)
        tab_hi = at("tab_hi", [P, 2 * TAB], F32R, AT_D + 13824)
        tab_lo = at("tab_lo", [P, 2 * TAB], F32R, AT_D + 14592)

        o_all = at("o_all", [P, UNITS, HD], F32, AT_B)
        prob = at("prob", [P, PRING, N], F32, AT_A)
        k_sb = at("k_sb", [P, 2, N], F32R, AT_C)
        v_sb = at("v_sb", [P, 2, NT, HD], F32, AT_C + 18432)
        p_t = at("p_t", [P, TRING, N], F32, AT_C + 27648)
        added = at("added", [P, BRING, N], F32, AT_C + 46080)
        q_sb = at("q_sb", [P, QRING, 2, P], F32R, AT_C + 73728)
        rel_sb = at("rel_sb", [P, QRING, TAB], F32, AT_C + 76800)

        wo_f = at("wo_f", [P, 2, KC, W], F32, AT_D)
        wo_hi = at("wo_hi", [P, 2, KC, W], F32R, AT_A)
        wo_lo = at("wo_lo", [P, 2, KC, W], F32R, AT_A + 18432)
        o_tile = at("o_tile", [P, 2, D], F32, AT_C)
        x_res = at("x_res", [P, 2, D], F32, AT_C + 6144)
        x_out = at("x_out", [P, 2, D], F32, AT_C + 12288)
        ot_hi = at("ot_hi", [P, 2, KC, P], F32R, AT_C + 18432)
        ot_lo = at("ot_lo", [P, 2, KC, P], F32R, AT_C + 24576)
        bo_sb = at("bo_sb", [P, D], F32, AT_C + 30720)

        ps = ctx.enter_context(nc.psum_tensor("ps", [P, 8, 512], F32))

        x_mid = nc.dram_tensor("x_mid", (N, D), F32, kind="Internal").ap()

        def layer(n):
            def dram(name, shape, dt):
                return nc.dram_tensor(f"{name}{n}", shape, dt, kind="Internal").ap()

            s = Layer()
            s.x_tr = sem(f"x_tr_{n}")
            s.norm_act = sem(f"norm_act_{n}")
            s.norm_dve = sem(f"norm_dve_{n}")
            s.stat_dve = sem(f"stat_dve_{n}")
            s.stat_mm = sem(f"stat_mm_{n}")
            s.root_done = sem(f"root_done_{n}")
            s.applied = sem(f"applied_{n}")
            s.hi_ready = sem(f"hi_ready_{n}")
            s.lo_ready = sem(f"lo_ready_{n}")
            s.small_in = sem(f"small_in_{n}")
            s.w_hi_done = sem(f"w_hi_done_{n}")
            s.w_lo_done = sem(f"w_lo_done_{n}")
            s.grp_mm = sem(f"grp_mm_{n}")
            s.e_hi_done = sem(f"e_hi_done_{n}")
            s.e_lo_done = sem(f"e_lo_done_{n}")
            s.v_f_done = sem(f"v_f_done_{n}")
            s.v_tr = sem(f"v_tr_{n}")
            s.v_n_done = sem(f"v_n_done_{n}")
            s.wo_in = sem(f"wo_in_{n}")
            s.k_in = sem(f"k_in_{n}")
            s.v_in = sem(f"v_in_{n}")
            s.scores = sem(f"scores_{n}")
            s.scores_read = sem(f"scores_read_{n}")
            s.nmax_done = sem(f"nmax_done_{n}")
            s.exp_done = sem(f"exp_done_{n}")
            s.p_tr = sem(f"p_tr_{n}")
            s.p_act = sem(f"p_act_{n}")
            s.p_dve = sem(f"p_dve_{n}")
            s.pv = sem(f"pv_{n}")
            s.rinv_done = sem(f"rinv_done_{n}")
            s.o_read = sem(f"o_read_{n}")
            s.turn_dve = sem(f"turn_dve_{n}")
            s.turn_act = sem(f"turn_act_{n}")
            s.turn_pool = sem(f"turn_pool_{n}")
            s.bo_in = sem(f"bo_in_{n}")
            s.wo_hi_done = sem(f"wo_hi_done_{n}")
            s.wo_lo_done = sem(f"wo_lo_done_{n}")
            s.o_tr = sem(f"o_tr_{n}")
            s.ot_hi_done = sem(f"ot_hi_done_{n}")
            s.ot_lo_done = sem(f"ot_lo_done_{n}")
            s.out_mm = sem(f"out_mm_{n}")
            s.out_res = sem(f"out_res_{n}")
            s.out_bias = sem(f"out_bias_{n}")
            if n == 0:
                s.lora_in = sem(f"lora_in_{n}")
                s.lora_mm = sem(f"lora_mm_{n}")
                s.lora_added = sem(f"lora_added_{n}")
                s.qr_mm = sem(f"qr_mm_{n}")
                s.qr_sb_done = sem(f"qr_sb_done_{n}")
                s.rel_out = sem(f"rel_out_{n}")
                s.add_ready = sem(f"add_ready_{n}")
            else:
                s.decay_pool = sem(f"decay_pool_{n}")
                s.decay_dve = sem(f"decay_dve_{n}")
            s.x_in = [sem(f"x_in{b}_{n}") for b in range(2)]
            s.w_in = [sem(f"w_in{b}_{n}") for b in range(2)]
            s.qkv_out = [sem(f"qkv_out{t}_{n}") for t in range(OT)]
            s.q_in = [sem(f"q_in{t}_{n}") for t in range(QRING)]
            s.add_in = [sem(f"add_in{t}_{n}") for t in range(BRING)]
            s.o_in = [sem(f"o_in{b}_{n}") for b in range(2)]
            s.out_st = [sem(f"out_st{b}_{n}") for b in range(2)]
            s.n = n
            s.rel = n == 0
            s.qd = dram("qd", (UNITS, HD, 2, P), F32)
            s.kd = dram("kd", (H, 2, HD, N), F32)
            s.vd = dram("vd", (H, P, NT, HD), F32)
            if s.rel:
                s.qr_out = [sem(f"qr_out{t}_{n}") for t in range(OT)]
                s.qr = dram("qr", (H, N, 2 * TAB), F32)
                s.rd = dram("rd", (UNITS * P, TAB), F32)
            s.x = x_in if s.rel else x_mid
            s.out = x_mid if s.rel else out
            s.evac = EVAC[n]
            s.n_act, s.n_dve = s.evac.count("A"), s.evac.count("D")
            return s

        layers = [layer(0), layer(1)]
        const_in = sem("const_in")
        tab_split = sem("tab_split")
        block = ctx.enter_context(nc.Block())

        SC_CREDIT = SCH * QRING

        def turns(eng, body):
            with eng.Fori(0, TURNS - 1) as g:
                body(g)
            body(TURNS - 1)

        def unit(g, j):
            g, j = g + j // UNROLL, j % UNROLL
            return None if isinstance(g, int) and g >= TURNS else (g, j)

        def head(g):
            return g // TPH

        def bank_pair(b):
            return ps[:, 2 * b:2 * b + 2, 0:W]

        def halves(ap):
            return ap.rearrange("p (a b) -> p a b", a=2)

        def group_bank(j, q):
            return 4 + (len(TGROUPS) * j + q) % 3

        def split_order(first, second):
            first(0)
            first(1)
            second(0)
            first(2)
            second(1)
            second(2)

        @block.sync
        def _(sp):
            sp.dma_start(ident[:], ident_in).then_inc(const_in, 16)
            sp.dma_start(avg[:], avg_in).then_inc(const_in, 16)
            sp.dma_start(spread[:], spread_in).then_inc(const_in, 16)
            sp.dma_start(tab_f[:], tables).then_inc(const_in, 16)

            for s in layers:
                for q in s.qkv_out + (s.qr_out if s.rel else []):
                    sp.sem_inc(q, 64)
                for q in s.out_st:
                    sp.sem_inc(q, 16)
            for s in layers:
                if not s.rel:
                    for q in layers[0].out_st:
                        sp.wait_ge(q, 16 * (NT // 2 + 1))
                sp.dma_start(bcol[:], b_qkv[s.n]).then_inc(s.small_in, 16)
                for half in range(2):
                    sp.dma_start(stage[:, half], w_all[s.n, half]).then_inc(s.w_in[half], 16)
                if s.rel:
                    sp.dma_start(la[:], lora_a[0]).then_inc(s.lora_in, 16)
                    sp.dma_start(lb[:], lora_b[0]).then_inc(s.lora_in, 16)
                with sp.Fori(0, NT // 2) as i:
                    for b in range(2):
                        sp.wait_ge(s.x_tr, 2 * i + b + 1)
                        sp.dma_start(x_tile[:, b], s.x[bass.ds((2 * i + b) * P, P), :]).then_inc(s.x_in[b], 16)

                for half in range(HALVES):
                    kind, pair0 = "qkv"[half // 2], (half % 2) * OT
                    if half + 2 < HALVES:
                        sp.wait_ge(s.w_hi_done, half + 1)
                        sp.wait_ge(s.w_lo_done, half + 1)
                        sp.dma_start(stage[:, half % 2], w_all[s.n, half + 2]).then_inc(s.w_in[half % 2], 16)
                    if s.rel and half in (0, 2):
                        sp.wait_ge(s.lora_mm, KC * (half + 2))
                        sp.dma_start(la[:], lora_a[half // 2 + 1]).then_inc(s.lora_in, 16)
                        sp.dma_start(lb[:], lora_b[half // 2 + 1]).then_inc(s.lora_in, 16)
                    if s.rel and half == 2:
                        for q in s.qr_out:
                            sp.wait_ge(q, 64 + 64 * 2 * NCH)
                    if half == HALVES - 1:
                        for wh in range(2):
                            sp.dma_start(wo_f[:, wh], w_all[s.n, HALVES + wh]).then_inc(s.wo_in, 16)
                    with sp.Fori(0, NCH) as c:
                        for t in range(OT):
                            group = half * NCH * OT + c * OT + t
                            heads = [2 * (pair0 + t) + hh for hh in range(2)]
                            if kind == "v":
                                sp.wait_ge(s.v_n_done, c * OT + (half - 4) * NCH * OT + t + 1 + OT)
                                for hh, h in enumerate(heads):
                                    sp.dma_start(s.vd[h][:, bass.ds(c * CT, CT), :],
                                                 v_n[:, t, :, hh * HD:(hh + 1) * HD]).then_inc(s.qkv_out[t], 32)
                                continue
                            for part, e in enumerate((e_hi, e_lo)):
                                if part == 0:
                                    sp.wait_ge(s.e_hi_done, group + 1)
                                else:
                                    sp.wait_ge(s.e_lo_done, group + 1 + OT)
                                for hh, h in enumerate(heads):
                                    src = e[hh * HD:(hh + 1) * HD, t, :].bitcast(F32)
                                    if kind == "q":
                                        dst = s.qd[bass.ds(c * CT + h * NT, CT), :, part, :].rearrange("t d n -> d t n")
                                        src = src.rearrange("d (t n) -> d t n", t=CT)
                                    else:
                                        dst = s.kd[h, part, :, bass.ds(c * W, W)]
                                    sp.dma_start(dst, src).then_inc(s.qkv_out[t], 16)
                            if s.rel and kind == "q":
                                sp.wait_ge(s.qr_sb_done, group + 1 + 1)
                                for hh, h in enumerate(heads):
                                    dst = s.qr[h, bass.ds(c * W, W), :].rearrange("(t p) n -> p t n", p=P)
                                    sp.dma_start(dst, qr_sb[:, t, hh * CT:(hh + 1) * CT, :]).then_inc(s.qr_out[t], 32)
                        if s.rel and kind == "k":
                            h = c + (half - 2) * NCH
                            products, dst = s.qr[h], s.rd[bass.ds(h * N, N), :].rearrange("(r c) n -> r c n", r=SIDE)
                            token, row = 2 * TAB, SIDE * 2 * TAB
                            for part, first, steps in ((0, SIDE - 1, (row - 1, token)), (1, TAB + SIDE - 1, (row, token - 1))):
                                src = bass.AP(products.tensor, products.offset + first,
                                              [[steps[0], SIDE], [steps[1], SIDE], [1, SIDE]])
                                sp.dma_start(dst[:, :, part * SIDE:(part + 1) * SIDE], src).then_inc(s.rel_out, 16)

                for t in range(OT):
                    sp.wait_ge(s.qkv_out[t], 64 + 64 * HALVES * NCH)
                if s.rel:
                    sp.wait_ge(s.rel_out, 16 * 2 * H)
                sp.dma_start(k_sb[:, 0].bitcast(F32), s.kd[0].rearrange("a d n -> (a d) n")).then_inc(s.k_in, 16)
                sp.dma_start(v_sb[:, 0], s.vd[0]).then_inc(s.v_in, 16)

                def loads(g):
                    for j in range(UNROLL):
                        u = UNROLL * g + j
                        sp.wait_ge(s.scores, SCH * u + SCH)
                        for part in range(2):
                            sp.dma_start(q_sb[part * HD:(part + 1) * HD, j % QRING].bitcast(F32), s.qd[u]).then_inc(s.q_in[j % QRING], 16)
                        if s.rel:
                            sp.wait_ge(s.add_ready, u + 1)
                            sp.dma_start(rel_sb[:, j % BRING], s.rd[bass.ds(u * P, P), :]).then_inc(s.add_in[j % BRING], 16)
                        else:
                            sp.wait_ge(s.decay_pool, u + 1)
                            sp.wait_ge(s.decay_dve, u + 1)
                            sp.dma_start(added[:, j % BRING], decay[bass.ds(u * P, P), :]).then_inc(s.add_in[j % BRING], 16)

                with sp.Fori(0, H - 1) as h:
                    with sp.Fori(0, TPH) as i:
                        loads(h * TPH + i)
                    sp.wait_ge(s.k_in, 16 * h + 16)
                    sp.wait_ge(s.v_in, 16 * h + 16)
                    sp.dma_start(k_sb[:, (h + 1) % 2].bitcast(F32), s.kd[h + 1].rearrange("a d n -> (a d) n")).then_inc(s.k_in, 16)
                    sp.dma_start(v_sb[:, (h + 1) % 2], s.vd[h + 1]).then_inc(s.v_in, 16)
                with sp.Fori(0, TPH) as i:
                    loads(i + (H - 1) * TPH)

                sp.wait_ge(s.pv, UNITS)
                sp.wait_ge(s.o_read, UNITS + 1)
                sp.dma_start(bo_sb[:], b_out[s.n].unsqueeze(0).to_broadcast([P, D])).then_inc(s.bo_in, 16)
                o_view = o_all[:].rearrange("p (h t) d -> p h t d", h=H)

                def tile_in(i, b):
                    sp.wait_ge(s.o_tr, 2 * i + b + 1)
                    sp.dma_start(o_tile[:, b].rearrange("p (h t d) -> p h t d", h=H, t=1),
                                 o_view[:, :, bass.ds(2 * i + b, 1), :]).then_inc(s.o_in[b], 16)
                    sp.wait_ge(s.out_res, 2 * i + b + 1)
                    sp.dma_start(x_res[:, b], s.x[bass.ds((2 * i + b) * P, P), :]).then_inc(s.o_in[b], 16)

                def tile_out(i, b):
                    sp.wait_ge(s.out_bias, 2 * i + b + 1)
                    sp.dma_start(s.out[bass.ds((2 * i + b) * P, P), :], x_out[:, b]).then_inc(s.out_st[b], 16)

                tile_in(0, 0)
                tile_in(0, 1)
                with sp.Fori(0, NT // 2 - 1) as i:
                    for b in range(2):
                        tile_out(i, b)
                        tile_in(i + 1, b)
                for b in range(2):
                    tile_out(NT // 2 - 1, b)
            for q in s.out_st:
                sp.wait_ge(q, 16 * (NT // 2 + 1))

        @block.tensor
        def _(pe):
            for s in layers:
                pe.sem_inc(s.x_tr, 2)
                pe.sem_inc(s.scores, SC_CREDIT)
                pe.sem_inc(s.v_tr, OT)
                pe.sem_inc(s.o_tr, 2)
                pe.sem_inc(s.out_mm, 2)
            pe.wait_ge(const_in, 64)
            for s in layers:
                def lora(half):
                    if not s.rel:
                        return
                    pe.wait_ge(s.lora_in, 32 * (half // 2 + 1))
                    for k in range(KC):
                        n = half * KC + k
                        pe.wait_ge(s.lora_added, n + 1)
                        pe.matmul(ps[:, 6 + k % 2, 0:W], la[:, k * P:(k + 1) * P],
                                  lb[:, (half % 2) * W:(half % 2 + 1) * W], start=True, stop=True).then_inc(s.lora_mm, 1)

                lora(0)
                lora(1)
                with pe.Fori(0, NT // 2) as i:
                    for b in range(2):
                        pe.wait_ge(s.x_in[b], 16 * i + 16)
                        pe.wait_ge((s.norm_act, s.norm_dve)[b], i + 1)
                        for k in range(KC):
                            mm = pe.transpose(ps[:, 2 * b + k // 3, (k % 3) * P:(k % 3 + 1) * P],
                                              x_tile[:, b, k * P:(k + 1) * P], ident[:])
                        mm.then_inc(s.x_tr, 1)

                def group_mean(bank, column):
                    for k in range(KC):
                        mm = pe.matmul(ps[0:GROUPS, bank, 0:1], avg[:, k, :], column(k), start=(k == 0), stop=(k == KC - 1))
                    mm.then_inc(s.stat_mm, 1)

                def to_channels(bank, value):
                    for k in range(KC):
                        mm = pe.matmul(ps[:, bank, 8 + k:9 + k], spread[:, k * P:(k + 1) * P], value, start=True, stop=True)
                    mm.then_inc(s.stat_mm, 1)

                pe.wait_ge(s.stat_dve, 1 + KC)
                group_mean(6, lambda k: mv[:, k, 0:1])
                pe.wait_ge(s.stat_dve, 2 + KC)
                to_channels(6, grp[:, 0:1])
                pe.wait_ge(s.stat_dve, 6 + KC)
                group_mean(7, lambda k: spread_var[:, k:k + 1])
                pe.wait_ge(s.stat_dve, 12 + KC)
                to_channels(7, grp[:, 7:8])

                for half in range(HALVES):
                    kind, w = "qkv"[half // 2], half % 2
                    if 1 <= half < HALVES - 1:
                        lora(half + 1)
                    pe.wait_ge(s.w_hi_done, half + 1)
                    pe.wait_ge(s.w_lo_done, half + 1)
                    if half == 0 and s.rel:
                        pe.wait_ge(tab_split, 2)
                    if half == 4:
                        pe.wait_ge(s.e_lo_done, 4 * NCH * OT + OT)
                    with pe.Fori(0, NCH) as c:
                        pe.wait_ge(s.hi_ready, c + 1)
                        pe.wait_ge(s.lo_ready, c + 1)

                        def product(t):
                            group = c * OT + half * NCH * OT + t
                            if kind == "v":
                                pe.wait_ge(s.v_f_done, group - 4 * NCH * OT + 1)
                            else:
                                pe.wait_ge(s.e_lo_done, group + 1)
                            for k in range(KC):
                                wt = slice(t * P, (t + 1) * P)
                                xc = bass.ds(c * W, W)
                                pe.matmul(ps[:, t, 0:W], w_hi[:, w, k, wt], x_hi[:, k, xc], start=(k == 0), stop=False)
                                pe.matmul(ps[:, t, 0:W], w_hi[:, w, k, wt], x_lo[:, k, xc], start=False, stop=False)
                                mm = pe.matmul(ps[:, t, 0:W], w_lo[:, w, k, wt], x_hi[:, k, xc], start=False, stop=(k == KC - 1))
                            mm.then_inc(s.grp_mm, 1)

                        def tables_or_turn(t):
                            group = c * OT + half * NCH * OT + t
                            if kind == "v":
                                n = group - 4 * NCH * OT
                                pe.wait_ge(s.v_n_done, n + 1)
                                pe.wait_ge(s.v_f_done, n + 1 + OT)
                                for tt in range(CT):
                                    mm = pe.transpose(ps[:, 3 + t, tt * P:(tt + 1) * P], v_f[:, t, tt * P:(tt + 1) * P], ident[:])
                                mm.then_inc(s.v_tr, 1)
                            elif s.rel and kind == "q":
                                pe.wait_ge(s.qr_sb_done, group + 1)
                                pe.wait_ge(s.e_lo_done, group + 1 + OT)
                                for hh in range(2):
                                    rows = slice(hh * HD, (hh + 1) * HD)
                                    if hh:
                                        pe.wait_ge(s.qr_mm, 2 * group + 1)
                                    for tt in range(CT):
                                        n, cols = hh * CT + tt, slice(tt * P, (tt + 1) * P)
                                        dst = ps[:, 3 + n // 2, (n % 2) * 2 * TAB:(n % 2 + 1) * 2 * TAB]
                                        pe.matmul(dst, e_hi[rows, t, cols], tab_hi[rows, :], start=True, stop=False)
                                        pe.matmul(dst, e_hi[rows, t, cols], tab_lo[rows, :], start=False, stop=False)
                                        mm = pe.matmul(dst, e_lo[rows, t, cols], tab_hi[rows, :], start=False, stop=True)
                                    mm.then_inc(s.qr_mm, 1)

                        split_order(product, tables_or_turn)

                def scores(at_unit, c):
                    if at_unit is None:
                        return
                    g, j = at_unit
                    u = UNROLL * g + j
                    if c == 0:
                        pe.wait_ge(s.q_in[j % QRING], 32 * (2 * g + j // QRING + 1))
                        pe.wait_ge(s.k_in, 16 * head(g) + 16)
                    pe.wait_ge(s.scores_read, SCH * u + c + 1)
                    pair = (SCH * j + c) % 2
                    for b in range(2):
                        for part in range(2):
                            mm = pe.matmul(ps[:, 2 * pair + b, 0:W], q_sb[:, j % QRING, part, :],
                                           k_sb[:, head(g) % 2, (2 * c + b) * W:(2 * c + b + 1) * W],
                                           start=(part == 0), stop=(part == 1))
                    mm.then_inc(s.scores, 1)

                def transposes(g, j, q):
                    u = UNROLL * g + j
                    if s.rel and q == 0:
                        pe.wait_ge(s.exp_done, u + 1)
                    if not s.rel and q == 0:
                        pe.wait_ge(s.decay_pool, u + 1 + BRING)
                    if not s.rel and q == 3:
                        pe.wait_ge(s.decay_dve, u + 1 + BRING)
                    before = (q - 3) % len(TGROUPS)
                    uu = u + (0 if q >= 3 else -1)
                    if s.evac[before] == "A":
                        pe.wait_ge(s.p_act, s.n_act * (uu + 1) + s.evac[:before + 1].count("A"))
                    else:
                        pe.wait_ge(s.p_dve, s.n_dve * (uu + 1) + s.evac[:before + 1].count("D"))
                    first = sum(TGROUPS[:q])
                    for m in range(TGROUPS[q]):
                        mm = pe.transpose(ps[:, group_bank(j, q), m * P:(m + 1) * P],
                                          prob[:, j % PRING, (first + m) * P:(first + m + 1) * P], ident[:])
                    mm.then_inc(s.p_tr, 1)

                def values(g, j):
                    u = UNROLL * g + j
                    pe.wait_ge(s.v_in, 16 * head(g) + 16)
                    pe.wait_ge(s.p_act, s.n_act * (u + 2))
                    pe.wait_ge(s.p_dve, s.n_dve * (u + 2))
                    pe.wait_ge(s.o_read, u + 1)
                    for m in range(NT):
                        mm = pe.matmul(ps[:, 7, 0:HD], p_t[:, j % TRING, m * P:(m + 1) * P], v_sb[:, head(g) % 2, m, :],
                                       start=(m == 0), stop=(m == NT - 1))
                    mm.then_inc(s.pv, 1)

                def attend(g):
                    for j in range(UNROLL):
                        for q in range(3):
                            transposes(g, j, q)
                        scores(unit(g, j + LAG), 0)
                        transposes(g, j, 3)
                        transposes(g, j, 4)
                        scores(unit(g, j + LAG), 1)
                        scores(unit(g, j + LAG), 2)
                        values(g, j)

                for j in range(LAG):
                    for c in range(SCH):
                        scores((0, j), c)
                turns(pe, attend)

                def turn(i, b):
                    pe.wait_ge(s.o_in[b], 32 * i + 32)
                    pe.wait_ge(s.ot_lo_done, 2 * i + b + 1)
                    for k in range(KC):
                        mm = pe.transpose(ps[:, 2 * b + k // 3, (k % 3) * P:(k % 3 + 1) * P],
                                          o_tile[:, b, k * P:(k + 1) * P], ident[:])
                    mm.then_inc(s.o_tr, 1)

                def project_out(i, b):
                    pe.wait_ge(s.ot_lo_done, 2 * i + b + 1 + 2)
                    pe.wait_ge(s.out_res, 2 * i + b + 1)
                    for wh in range(2):
                        dst = ps[:, 4 + 2 * b + wh, 0:W]
                        for k in range(KC):
                            pe.matmul(dst, ot_hi[:, b, k, :], wo_hi[:, wh, k, :], start=(k == 0), stop=False)
                            pe.matmul(dst, ot_hi[:, b, k, :], wo_lo[:, wh, k, :], start=False, stop=False)
                            mm = pe.matmul(dst, ot_lo[:, b, k, :], wo_hi[:, wh, k, :], start=False, stop=(k == KC - 1))
                    mm.then_inc(s.out_mm, 1)

                turn(0, 0)
                pe.wait_ge(s.wo_hi_done, 1)
                pe.wait_ge(s.wo_lo_done, 1)
                with pe.Fori(0, NT // 2 - 1) as i:
                    turn(i, 1)
                    project_out(i, 0)
                    turn(i + 1, 0)
                    project_out(i, 1)
                turn(NT // 2 - 1, 1)
                project_out(NT // 2 - 1, 0)
                project_out(NT // 2 - 1, 1)

        @block.scalar
        def _(act):
            for s in layers:
                act.sem_inc(s.norm_act, 1)
                act.sem_inc(s.v_f_done, OT)
                act.sem_inc(s.p_act, s.n_act)
                if s.rel:
                    act.sem_inc(s.qr_sb_done, 1)
            for s in layers:
                def split_weights(half):
                    if s.rel:
                        act.wait_ge(s.lora_added, KC * (half + 1) + 2)
                    else:
                        act.wait_ge(s.w_in[half % 2], 16 * (half // 2 + 1))
                    if half >= 2:
                        act.wait_ge(s.grp_mm, (half - 1) * NCH * OT)
                    nc.scalar.activation(w_hi[:, half % 2], stage[:, half % 2], ACT.Copy,
                                         scale=SCALE if half // 2 == 1 else 1.0).then_inc(s.w_hi_done, 1)

                split_weights(0)
                split_weights(1)
                with act.Fori(0, NT // 2) as i:
                    act.wait_ge(s.x_tr, 2 * i + 1 + 2)
                    act.sem_inc(s.turn_act, 1)
                    nc.scalar.activation(x_t[:, :, bass.ds(2 * i * P, P)].rearrange("p (a b) n -> p a b n", a=2),
                                         bank_pair(0).rearrange("p a (b n) -> p a b n", b=3), ACT.Copy).then_inc(s.norm_act, 1)
                act.wait_ge(s.stat_dve, 7 + KC)
                nc.scalar.activation(grp[:, 2:3], grp[:, 1:2], ACT.Sqrt).then_inc(s.root_done, 1)
                with act.Fori(0, NCH) as c:
                    act.wait_ge(s.applied, c + 1)
                    act.sem_inc(s.turn_act, 1)
                    nc.scalar.activation(x_hi[:, :, bass.ds(c * W, W)], x_t[:, :, bass.ds(c * W, W)], ACT.Copy).then_inc(s.hi_ready, 1)

                for half in range(HALVES):
                    kind = "qkv"[half // 2]
                    if 1 <= half < HALVES - 1:
                        split_weights(half + 1)
                    if half == 4:
                        for q in s.qkv_out:
                            act.wait_ge(q, 64 + 64 * 4 * NCH)
                    with act.Fori(0, NCH) as c:
                        def part(t):
                            group = c * OT + half * NCH * OT + t
                            bias = bcol[:, (half // 2) * KC + (half % 2) * OT + t:][:, 0:1]
                            act.wait_ge(s.grp_mm, group + 1)
                            if kind == "v":
                                act.wait_ge(s.v_tr, group - 4 * NCH * OT + 1)
                                nc.scalar.activation(v_f[:, t, :], ps[:, t, 0:W], ACT.Identity, bias=bias).then_inc(s.v_f_done, 1)
                            else:
                                act.wait_ge(s.qkv_out[t], 64 * (c + half * NCH + 1))
                                nc.scalar.activation(e_hi[:, t, :], ps[:, t, 0:W], ACT.Identity, bias=bias).then_inc(s.e_hi_done, 1)

                        def products(t):
                            if not (s.rel and kind == "q"):
                                return
                            act.wait_ge(s.qr_mm, 2 * (c * OT + half * NCH * OT + t) + 2)
                            act.wait_ge(s.qr_out[t], 64 * (c + half * NCH + 1))
                            nc.scalar.activation(qr_sb[:, t].rearrange("p (a b) n -> p a (b n)", a=3),
                                                 ps[:, 3:6, 0:W], ACT.Copy).then_inc(s.qr_sb_done, 1)

                        split_order(part, products)

                def exponentials(at_unit):
                    if at_unit is None:
                        return
                    g, j = at_unit
                    act.wait_ge(s.nmax_done, UNROLL * g + j + 1 + BRING)
                    r = j % PRING
                    nc.scalar.activation(prob[:, r, :], prob[:, r, :], ACT.Exp, bias=nmax[:, r:r + 1],
                                         accum_out=rsum[:, r:r + 1]).then_inc(s.exp_done, 1)

                def attend(g):
                    for j in range(UNROLL):
                        for q in range(len(TGROUPS)):
                            if s.evac[q] == "A":
                                act.wait_ge(s.p_tr, len(TGROUPS) * (UNROLL * g + j) + q + 1)
                                first, n = sum(TGROUPS[:q]) * P, TGROUPS[q] * P
                                nc.scalar.activation(p_t[:, j % TRING, first:first + n], ps[:, group_bank(j, q), 0:n],
                                                     ACT.Copy).then_inc(s.p_act, 1)
                        exponentials(unit(g, j + XLAG))

                for j in range(XLAG):
                    exponentials((0, j))
                turns(act, attend)

                act.wait_ge(s.wo_in, 32)
                act.wait_ge(s.pv, UNITS)
                nc.scalar.activation(wo_hi[:], wo_f[:], ACT.Copy).then_inc(s.wo_hi_done, 1)
                with act.Fori(0, NT // 2) as i:
                    for b in range(2):
                        act.wait_ge(s.o_tr, 2 * i + b + 1 + 2)
                        act.wait_ge(s.out_mm, 2 * i + b + 1)
                        nc.scalar.activation(ot_hi[:, b].rearrange("p (a k) n -> p a (k n)", a=2), bank_pair(b),
                                             ACT.Copy).then_inc(s.ot_hi_done, 1)

        @block.vector
        def _(dve):
            for s in layers:
                dve.sem_inc(s.norm_dve, 1)
                dve.sem_inc(s.e_lo_done, OT)
                dve.sem_inc(s.v_n_done, OT)
                dve.sem_inc(s.scores_read, 2)
                dve.sem_inc(s.nmax_done, BRING)
                dve.sem_inc(s.p_dve, s.n_dve)
                dve.sem_inc(s.o_read, 1)
                dve.sem_inc(s.ot_lo_done, 2)
                dve.sem_inc(s.out_res, 2)
                if s.rel:
                    dve.sem_inc(s.lora_added, 2)
                else:
                    dve.sem_inc(s.decay_dve, BRING)
            dve.wait_ge(const_in, 64)
            nc.vector.tensor_copy(tab_hi[:], tab_f[:]).then_inc(tab_split, 1)
            dve.wait_ge(tab_split, 1)
            nc.vector.tensor_tensor(tab_lo[:], tab_f[:], tab_hi[:].bitcast(F32), ALU.subtract).then_inc(tab_split, 1)

            for s in layers:
                def split_weights(half):
                    st = stage[:, half % 2]
                    dve.wait_ge(s.w_in[half % 2], 16 * (half // 2 + 1))
                    if s.rel:
                        for k in range(KC):
                            dve.wait_ge(s.lora_mm, half * KC + k + 1)
                            nc.vector.scalar_tensor_tensor(st[:, k, :], ps[:, 6 + k % 2, 0:W], LORA_SCALE, st[:, k, :],
                                                           ALU.mult, ALU.add).then_inc(s.lora_added, 1)
                    dve.wait_ge(s.w_hi_done, half + 1)
                    if s.rel:
                        dve.wait_ge(s.lora_added, KC * (half + 1) + 2)
                    nc.vector.scalar_tensor_tensor(w_lo[:, half % 2], st, SCALE if half // 2 == 1 else 1.0,
                                                   w_hi[:, half % 2].bitcast(F32), ALU.mult, ALU.subtract).then_inc(s.w_lo_done, 1)

                steps = [0]

                def stat(instruction):
                    steps[0] += 1
                    instruction.then_inc(s.stat_dve, 1)

                dve.wait_ge(s.small_in, 16)
                stat(nc.vector.tensor_scalar(bcol[:, KC:2 * KC], bcol[:, KC:2 * KC], SCALE, None, ALU.mult))
                split_weights(0)
                split_weights(1)
                with dve.Fori(0, NT // 2) as i:
                    dve.wait_ge(s.x_tr, 2 * i + 2 + 2)
                    nc.vector.tensor_scalar(x_t[:, :, bass.ds((2 * i + 1) * P, P)].rearrange("p (a b) n -> p a b n", a=2),
                                            bank_pair(1).rearrange("p a (b n) -> p a b n", b=3), 1.0, None,
                                            ALU.mult).then_inc(s.norm_dve, 1)
                    dve.wait_ge(s.norm_act, i + 1 + 1)
                    dve.wait_ge(s.norm_dve, i + 1 + 1)
                    dve.sem_inc(s.turn_dve, 1)
                    for k in range(KC):
                        last = nc.vector.bn_stats(bn[:, k, bass.ds(i, 1), :].rearrange("p a b -> p (a b)"), x_t[:, k, bass.ds(2 * i * P, 2 * P)])
                    last.then_inc(s.turn_dve, 1)
                dve.wait_ge(s.turn_dve, NT)
                for k in range(KC):
                    stat(nc.vector.bn_aggr(mv[:, k, :], bn[:, k].rearrange("p a b -> p (a b)")))
                dve.wait_ge(s.stat_mm, 1)
                stat(nc.vector.tensor_copy(grp[:, 0:1], ps[0:GROUPS, 6, 0:1]))
                dve.wait_ge(s.stat_mm, 2)
                stat(nc.vector.tensor_copy(mean_c[:], ps[:, 6, 8:8 + KC]))
                dve.wait_ge(s.stat_dve, steps[0])
                stat(nc.vector.tensor_tensor(dev[:], mv[:, :, 0], mean_c[:], ALU.subtract))
                dve.wait_ge(s.stat_dve, steps[0])
                stat(nc.vector.tensor_tensor(dev[:], dev[:], dev[:], ALU.mult))
                dve.wait_ge(s.stat_dve, steps[0])
                stat(nc.vector.tensor_tensor(spread_var[:], dev[:], mv[:, :, 1], ALU.add))
                assert steps[0] == 6 + KC
                dve.wait_ge(s.stat_mm, 3)
                stat(nc.vector.tensor_scalar(grp[:, 1:2], ps[0:GROUPS, 7, 0:1], EPS, None, ALU.add))
                dve.wait_ge(s.root_done, 1)
                stat(nc.vector.reciprocal(grp[:, 3:4], grp[:, 2:3]))
                dve.wait_ge(s.stat_dve, steps[0])
                stat(nc.vector.tensor_tensor(grp[:, 4:5], grp[:, 3:4], grp[:, 3:4], ALU.mult))
                dve.wait_ge(s.stat_dve, steps[0])
                stat(nc.vector.tensor_tensor(grp[:, 5:6], grp[:, 4:5], grp[:, 1:2], ALU.mult))
                dve.wait_ge(s.stat_dve, steps[0])
                stat(nc.vector.tensor_scalar(grp[:, 6:7], grp[:, 5:6], -0.5, 1.5, ALU.mult, ALU.add))
                dve.wait_ge(s.stat_dve, steps[0])
                stat(nc.vector.tensor_tensor(grp[:, 7:8], grp[:, 6:7], grp[:, 3:4], ALU.mult))
                assert steps[0] == 12 + KC
                dve.wait_ge(s.stat_mm, 4)
                stat(nc.vector.tensor_copy(rstd_c[:], ps[:, 7, 8:8 + KC]))
                dve.wait_ge(s.stat_dve, steps[0])
                with dve.Fori(0, NCH) as c:
                    for k in range(KC):
                        xc = x_t[:, k, bass.ds(c * W, W)]
                        last = nc.vector.tensor_scalar(xc, xc, mean_c[:, k:k + 1], rstd_c[:, k:k + 1], ALU.subtract, ALU.mult)
                    last.then_inc(s.applied, 1)

                for half in range(HALVES):
                    kind = "qkv"[half // 2]
                    if 1 <= half < HALVES - 1:
                        split_weights(half + 1)
                    with dve.Fori(0, NCH) as c:
                        def part(t):
                            group = c * OT + half * NCH * OT + t
                            if kind == "v":
                                return
                            bias = bcol[:, (half // 2) * KC + (half % 2) * OT + t:][:, 0:1]
                            dve.wait_ge(s.e_hi_done, group + 1)
                            dve.wait_ge(s.qkv_out[t], 64 * (c + half * NCH + 1))
                            nc.vector.scalar_tensor_tensor(e_lo[:, t, :], ps[:, t, 0:W], bias, e_hi[:, t, :].bitcast(F32),
                                                           ALU.add, ALU.subtract).then_inc(s.e_lo_done, 1)

                        def turned(t):
                            if kind != "v":
                                return
                            dve.wait_ge(s.v_tr, c * OT + (half - 4) * NCH * OT + t + 1 + OT)
                            dve.wait_ge(s.qkv_out[t], 64 * (c + half * NCH + 1))
                            nc.vector.tensor_copy(v_n[:, t].rearrange("p a n -> p (a n)"), ps[:, 3 + t, 0:W]).then_inc(s.v_n_done, 1)

                        split_order(part, turned)

                def score_copy(at_unit, c):
                    if at_unit is None:
                        return
                    g, j = at_unit
                    u, r = UNROLL * g + j, j % PRING
                    dve.wait_ge(s.scores, SCH * u + c + 1 + SC_CREDIT)
                    cols = slice(c * SC, (c + 1) * SC)
                    src = bank_pair((SCH * j + c) % 2)
                    dst = halves(prob[:, r, cols])
                    if s.rel:
                        if c == 0:
                            dve.wait_ge(s.add_ready, u + 1 + BRING)
                        dve.sem_inc(s.turn_dve, 1)
                        nc.vector.tensor_tensor_reduce(out=dst, in0=src, in1=halves(added[:, j % BRING, cols]), scale=1.0,
                                                       scalar=-BIG, op0=ALU.add, op1=ALU.max,
                                                       accum_out=pmax[:, r, c:c + 1]).then_inc(s.scores_read, 1)
                    else:
                        nc.vector.tensor_scalar(dst, src, 1.0, -BIG, ALU.mult, ALU.max,
                                                accum_out=pmax[:, r, c:c + 1]).then_inc(s.scores_read, 1)

                def row_max(at_unit):
                    if at_unit is None:
                        return
                    g, j = at_unit
                    r = j % PRING
                    dve.wait_ge(s.scores_read, SCH * (UNROLL * g + j) + SCH + 2)
                    nc.vector.tensor_reduce(nmax[:, r:r + 1], pmax[:, r, 0:SCH], AX, ALU.max, negate=True).then_inc(s.nmax_done, 1)

                def decays(at_unit):
                    if s.rel or at_unit is None:
                        return
                    g, j = at_unit
                    dve.wait_ge(s.exp_done, UNROLL * g + j + 1)
                    dve.wait_ge(s.add_in[j % BRING], 16 * (2 * g + j // BRING + 1))
                    pr = prob[:, j % PRING, POOL_COLS:N]
                    nc.vector.tensor_tensor(pr, pr, added[:, j % BRING, POOL_COLS:N], ALU.mult).then_inc(s.decay_dve, 1)

                def turned_out(at_unit, q):
                    if at_unit is None or s.evac[q] != "D":
                        return
                    g, j = at_unit
                    dve.wait_ge(s.p_tr, len(TGROUPS) * (UNROLL * g + j) + q + 1)
                    first, n = sum(TGROUPS[:q]) * P, TGROUPS[q] * P
                    nc.vector.tensor_copy(p_t[:, j % TRING, first:first + n], ps[:, group_bank(j, q), 0:n]).then_inc(s.p_dve, 1)

                def normalise(g, j):
                    u, r = UNROLL * g + j, j % PRING
                    dve.wait_ge(s.exp_done, u + 1)
                    nc.vector.reciprocal(rinv[:, r:r + 1], rsum[:, r:r + 1]).then_inc(s.rinv_done, 1)
                    dve.wait_ge(s.rinv_done, u + 1)
                    dve.wait_ge(s.pv, u + 1)
                    nc.vector.tensor_scalar(o_all[:, bass.ds(u, 1), :].rearrange("p a d -> p (a d)"), ps[:, 7, 0:HD],
                                            rinv[:, r:r + 1], None, ALU.mult).then_inc(s.o_read, 1)

                def attend(g):
                    for j in range(UNROLL):
                        ahead = unit(g, j + LAG)
                        score_copy(ahead, 0)
                        turned_out((g, j), 3)
                        score_copy(ahead, 1)
                        score_copy(ahead, 2)
                        row_max(ahead)
                        decays(unit(g, j + MLAG))
                        turned_out(unit(g, j + 1), 1)
                        normalise(g, j)

                for j in range(LAG):
                    for c in range(SCH):
                        score_copy((0, j), c)
                    row_max((0, j))
                for j in range(MLAG):
                    decays((0, j))
                turned_out((0, 0), 1)
                turns(dve, attend)

                dve.wait_ge(s.wo_in, 32)
                dve.wait_ge(s.wo_hi_done, 1)
                nc.vector.tensor_tensor(wo_lo[:], wo_f[:], wo_hi[:].bitcast(F32), ALU.subtract).then_inc(s.wo_lo_done, 1)

                def low(i, b):
                    dve.wait_ge(s.ot_hi_done, 2 * i + b + 1)
                    nc.vector.tensor_tensor(ot_lo[:, b].rearrange("p (a k) n -> p a (k n)", a=2), bank_pair(b),
                                            ot_hi[:, b].rearrange("p (a k) n -> p a (k n)", a=2).bitcast(F32),
                                            ALU.subtract).then_inc(s.ot_lo_done, 1)

                def residual(i, b):
                    dve.wait_ge(s.out_mm, 2 * i + b + 1 + 2)
                    dve.wait_ge(s.o_in[b], 32 * i + 32)
                    dve.wait_ge(s.out_st[b], 16 * i + 16)
                    nc.vector.tensor_tensor(halves(x_out[:, b, :]), bank_pair(2 + b), halves(x_res[:, b, :]),
                                            ALU.add).then_inc(s.out_res, 1)

                low(0, 0)
                with dve.Fori(0, NT // 2 - 1) as i:
                    low(i, 1)
                    residual(i, 0)
                    low(i + 1, 0)
                    residual(i, 1)
                low(NT // 2 - 1, 1)
                residual(NT // 2 - 1, 0)
                residual(NT // 2 - 1, 1)

        @block.gpsimd
        def _(pool):
            pool.sem_inc(layers[0].add_ready, BRING)
            pool.sem_inc(layers[1].decay_pool, BRING)
            for s in layers:
                with pool.Fori(0, NCH) as c:
                    pool.wait_ge(s.hi_ready, c + 1)
                    pool.sem_inc(s.turn_pool, 1)
                    xc = bass.ds(c * W, W)
                    nc.gpsimd.tensor_tensor(x_lo[:, :, xc], x_t[:, :, xc], x_hi[:, :, xc].bitcast(F32),
                                            ALU.subtract).then_inc(s.lo_ready, 1)
                with pool.Fori(0, TURNS) as g:
                    for j in range(UNROLL):
                        u, b = UNROLL * g + j, j % BRING
                        pool.wait_ge(s.add_in[b], 16 * (2 * g + j // BRING + 1))
                        if s.rel:
                            pool.wait_ge(s.nmax_done, u + 1)
                            nc.gpsimd.tensor_tensor(added[:, b, :].rearrange("p (r c) -> p r c", r=SIDE),
                                                    rel_sb[:, b, 0:SIDE].unsqueeze(2).to_broadcast([P, SIDE, SIDE]),
                                                    rel_sb[:, b, SIDE:TAB].unsqueeze(1).to_broadcast([P, SIDE, SIDE]),
                                                    ALU.add).then_inc(s.add_ready, 1)
                        else:
                            pool.wait_ge(s.exp_done, u + 1)
                            pr = prob[:, j % PRING, 0:POOL_COLS]
                            nc.gpsimd.tensor_tensor(pr, pr, added[:, b, 0:POOL_COLS], ALU.mult).then_inc(s.decay_pool, 1)
                pool.wait_ge(s.bo_in, 16)
                with pool.Fori(0, NT // 2) as i:
                    for b in range(2):
                        pool.wait_ge(s.out_res, 2 * i + b + 1 + 2)
                        nc.gpsimd.tensor_tensor(x_out[:, b, :], x_out[:, b, :], bo_sb[:], ALU.add).then_inc(s.out_bias, 1)


def kernel(**inputs):
    import concourse.bacc as bacc
    from concourse.bass_utils import run_bass_kernel_spmd

    x = np.asarray(inputs["x"])
    f = x.dtype

    def get(name):
        return np.asarray(inputs[name])

    def halves_of(*weights):
        t = np.concatenate([w.T for w in weights], axis=1)
        return t.reshape(KC, P, -1, W).transpose(2, 1, 0, 3)

    q = "L0_conv_"
    r = "L1_conv_"
    w_all = np.ascontiguousarray(np.stack([
        halves_of(get(q + "qkv_w"), get(q + "proj_w")),
        halves_of(get(r + "Wq"), get(r + "Wk"), get(r + "Wv"), get(r + "Wo"))]))
    b_qkv = np.ascontiguousarray(np.stack([
        get(q + "qkv_b").reshape(3 * KC, P).T,
        np.concatenate([get(r + "bq"), get(r + "bk"), get(r + "bv")]).reshape(3 * KC, P).T]))
    b_out = np.ascontiguousarray(np.stack([get(q + "proj_b"), get(r + "bo")]))
    tables = np.zeros((2, HD, 2 * TAB), f)
    for k, name in enumerate(("rel_pos_h", "rel_pos_w")):
        tables[:, :, k * TAB:k * TAB + 2 * SIDE - 1] = get(q + name)[::-1].T
    group = np.arange(D) // GC
    member = group[:, None] == np.arange(GROUPS)[None, :]
    avg = np.ascontiguousarray((member / GC).astype(f).reshape(KC, P, GROUPS).transpose(1, 0, 2))
    arrays = {
        "x_in": np.ascontiguousarray(x.reshape(N, D)),
        "tables": tables.reshape(P, 2 * TAB),
        "lora_a": np.ascontiguousarray(np.stack([get(f"{q}lora_{m}_A") for m in "qkv"])),
        "lora_b": np.ascontiguousarray(np.stack([get(f"{q}lora_{m}_B").T for m in "qkv"])),
        "decay": np.ascontiguousarray(get(r + "decay").reshape(UNITS * P, N)),
        "w_all": w_all,
        "b_qkv": b_qkv,
        "b_out": b_out,
        "ident_in": np.eye(P, dtype=f),
        "avg_in": avg,
        "spread_in": np.ascontiguousarray(member.T.astype(f)),
    }
    nc = bacc.Bacc("TRN2", target_bir_lowering=False, num_devices=1, dynamic_dma_scratch_size=1024)
    args = {k: nc.dram_tensor(k, a.shape, mybir.dt.from_np(a.dtype), kind="ExternalInput").ap() for k, a in arrays.items()}
    args["out"] = nc.dram_tensor("out", (N, D), F32, kind="ExternalOutput").ap()
    program(nc, **args)
    got = run_bass_kernel_spmd(nc, [arrays], core_ids=[0])
    return got.results[0]["out"].reshape(x.shape)
```
